# Optimizing a Trainium2 kernel written in Bass

```python
import numpy as np
import jax
import jax.numpy as jnp

def _softmax(x, axis=-1):
    return jax.nn.softmax(x, axis=axis)

def _gelu(x):
    return jax.nn.gelu(x, approximate=True)

def _silu(x):
    return jax.nn.silu(x)

def _sigmoid(x):
    return jax.nn.sigmoid(x)

def _layernorm(x, axis=-1, eps=1e-05):
    m = jnp.mean(x, axis=axis, keepdims=True)
    v = jnp.var(x, axis=axis, keepdims=True)
    return (x - m) / jnp.sqrt(v + eps)

def _scatter_add(tgt, idx, src, axis=0):
    return tgt.at[idx].add(src)

def _segment_sum(src, seg, n):
    return jax.ops.segment_sum(src, seg, n)
kernel_name = 'mk_adj_preln_d1_adj_r2_1b1718'

def setup_inputs(seed: int=0):
    np.random.seed(seed)
    _w = jnp.asarray

    def _rec_inputs():
        import jax
        import jax.numpy as jnp
        _gk = jax.random.key(seed)
        x = -0.0001538 + 1 * jax.random.normal(jax.random.fold_in(_gk, 1), (128, 128, 384), jnp.float32)
        _a = jax.random.bernoulli(jax.random.fold_in(_gk, 2), 0.125, (128, 128, 128))
        _a = jnp.logical_or(_a, jnp.swapaxes(_a, -1, -2))
        _a = jnp.logical_or(_a, jnp.eye(128, dtype=bool))
        adj = _a
        return (x, adj)
    x, adj = _rec_inputs()

    def _L0_gnn_setup():
        import jax, jax.numpy as jnp
        import numpy as np
        B, S, H = (4, 1024, 384)
        NUM_HEADS = 6
        HEAD_SIZE = H // NUM_HEADS
        NEG = -9000000000000000.0

        def _heads(x):
            b, s, _ = x.shape
            return x.reshape(b, s, NUM_HEADS, HEAD_SIZE).transpose(0, 2, 1, 3)
        key = jax.random.key(seed)
        ks = jax.random.split(key, 10)
        seq_inputs = jax.random.normal(ks[0], (B, S, H), dtype=jnp.float32)
        gm = jax.random.randint(ks[1], (B, S, S), 0, 2) > 0
        graph_mask = gm | jnp.eye(S, dtype=bool)[None]
        sc = 1.0 / np.sqrt(H)
        Wq = jax.random.normal(ks[2], (H, H), dtype=jnp.float32) * sc
        bq = jnp.zeros((H,), dtype=jnp.float32)
        Wk = jax.random.normal(ks[3], (H, H), dtype=jnp.float32) * sc
        bk = jnp.zeros((H,), dtype=jnp.float32)
        Wv = jax.random.normal(ks[4], (H, H), dtype=jnp.float32) * sc
        bv = jnp.zeros((H,), dtype=jnp.float32)
        Wf = jax.random.normal(ks[5], (H, H), dtype=jnp.float32) * sc
        bf = jnp.zeros((H,), dtype=jnp.float32)
        return {'seq_inputs': seq_inputs, 'Wq': Wq, 'bq': bq, 'Wk': Wk, 'bk': bk, 'Wv': Wv, 'bv': bv, 'Wf': Wf, 'bf': bf, 'graph_mask': graph_mask}
    _L0_gnn_all = _L0_gnn_setup()
    _L0_gnn_in = {k: v for k, v in _L0_gnn_all.items() if k in ('Wq', 'bq', 'Wk', 'bk', 'Wv', 'bv', 'Wf', 'bf')}
    del _L0_gnn_all
    return {'x': x, 'adj': adj, 'L0_gnn_Wq': _L0_gnn_in['Wq'], 'L0_gnn_bq': _L0_gnn_in['bq'], 'L0_gnn_Wk': _L0_gnn_in['Wk'], 'L0_gnn_bk': _L0_gnn_in['bk'], 'L0_gnn_Wv': _L0_gnn_in['Wv'], 'L0_gnn_bv': _L0_gnn_in['bv'], 'L0_gnn_Wf': _L0_gnn_in['Wf'], 'L0_gnn_bf': _L0_gnn_in['bf']}

def reference(x, adj, L0_gnn_Wq, L0_gnn_bq, L0_gnn_Wk, L0_gnn_bk, L0_gnn_Wv, L0_gnn_bv, L0_gnn_Wf, L0_gnn_bf):
    import jax
    import jax.numpy as jnp

    def _L0_gnn_ref(seq_inputs, Wq, bq, Wk, bk, Wv, bv, Wf, bf, graph_mask):
        import jax, jax.numpy as jnp
        import numpy as np
        B, S, H = (4, 1024, 384)
        NUM_HEADS = 6
        HEAD_SIZE = H // NUM_HEADS
        NEG = -9000000000000000.0

        def _heads(x):
            b, s, _ = x.shape
            return x.reshape(b, s, NUM_HEADS, HEAD_SIZE).transpose(0, 2, 1, 3)
        q = _heads(seq_inputs @ Wq + bq)
        k = _heads(seq_inputs @ Wk + bk)
        v = _heads(seq_inputs @ Wv + bv)
        scores = jnp.einsum('bhqd,bhkd->bhqk', q, k) / np.sqrt(HEAD_SIZE)
        bias = jnp.where(graph_mask, 0.0, NEG)[:, None]
        probs = jax.nn.softmax(scores + bias, axis=-1)
        ctx = jnp.einsum('bhqk,bhkd->bhqd', probs, v)
        ctx = ctx.transpose(0, 2, 1, 3).reshape(seq_inputs.shape[0], seq_inputs.shape[1], H)
        return ctx @ Wf + bf
    h = jnp.maximum(_layernorm(x, axis=-1), 0.0)
    x = x + _L0_gnn_ref(h, L0_gnn_Wq, L0_gnn_bq, L0_gnn_Wk, L0_gnn_bk, L0_gnn_Wv, L0_gnn_bv, L0_gnn_Wf, L0_gnn_bf, adj)
    return x

_drawn_inputs = setup_inputs


def setup_inputs(seed=0):
    import zlib

    import numpy as np

    out = dict(_drawn_inputs(seed))
    spreads = {'L0_gnn_bq': (0.0, 0.8),
     'L0_gnn_bk': (0.0, 0.8),
     'L0_gnn_bv': (0.0, 0.1),
     'L0_gnn_bf': (0.0, 0.1)}
    factors = {}
    for name, (base, spread) in spreads.items():
        noise = np.random.default_rng([zlib.crc32(name.encode()), seed]).standard_normal(out[name].shape)
        drawn = base * np.exp(spread * noise) if base else spread * noise
        out[name] = jnp.asarray(drawn.astype(out[name].dtype))
    for name, factor in factors.items():
        out[name] = (out[name] * factor).astype(out[name].dtype)
    return out
```

```python
from contextlib import ExitStack

import concourse.bass as bass
from concourse import mybir

F32 = mybir.dt.float32
F32R = mybir.dt.float32r
U8 = mybir.dt.uint8
ALU = mybir.AluOpType
ACT = mybir.ActivationFunctionType
AX = mybir.AxisListType

GRAPHS, NODES, FEAT = 128, 128, 384
HEADS, HEAD = 6, 64
PAIRS = HEADS // 2
KT = FEAT // 128
GROUP = 4
COLS = GROUP * NODES
TILES = 2 * PAIRS
RING = 2 * GROUP
NEG = -9000000000000000.0
EPS = 1e-5
SCALE = 1.0 / HEAD ** 0.5

LOAD, STATS, NORM, LATE = 12, 9, 8, 2
XB = 6
FIRST, LOOP_END = 4, 116


def graph_attention(nc, x, adj, Wq, bq, Wk, bk, Wv, bv, Wf, bf, out):
    ctx = ExitStack()
    with ctx:
        def sb(name, shape, dt=F32):
            return ctx.enter_context(nc.sbuf_tensor(name, shape, dt))

        def ps(name, shape):
            return ctx.enter_context(nc.psum_tensor(name, shape, F32))

        def sem(name):
            return ctx.enter_context(nc.semaphore(name))

        w_raw = {n: sb(f"w_raw_{n}", [128, KT, FEAT]) for n in "qkvf"}
        w_hi = {n: sb(f"w_hi_{n}", [128, KT, FEAT], F32R) for n in "qkvf"}
        w_lo = {n: sb(f"w_lo_{n}", [128, KT, FEAT], F32R) for n in "qkvf"}
        qk_bias = sb("qk_bias", [128, 2, PAIRS])
        bv_col = sb("bv_col", [128, KT])
        bv_wide = sb("bv_wide", [128, KT, 128])
        bf_row = sb("bf_row", [1, FEAT])
        out_bias = sb("out_bias", [128, FEAT])
        ident = sb("ident", [128, 128])
        ones = sb("ones", [128, 128])
        minus_half = sb("minus_half", [128, 1])
        x_in = sb("x_in", [128, RING, FEAT])
        x_bias = sb("x_bias", [128, RING, FEAT])
        adj_in = sb("adj_in", [128, 2, GROUP, NODES], U8)
        mask = sb("mask", [128, 2, NODES])
        stats = sb("stats", [128, 2, 6])
        moments = sb("moments", [128, 2, 2])
        rstd = sb("rstd", [128, 2, 2])
        shift = sb("shift", [128, 2, 2])
        h = sb("h", [128, 2, FEAT])
        ht_hi = sb("ht_hi", [128, 2, KT, COLS], F32R)
        ht_lo = sb("ht_lo", [128, 2, KT, COLS], F32R)
        qk = sb("qk", [128, 2, TILES, COLS])
        v = sb("v", [128, 2, GROUP, FEAT])
        s = sb("s", [128, 2, HEADS, NODES])
        neg_max = sb("neg_max", [128, 2, HEADS])
        sums = sb("sums", [128, 2, HEADS])
        inv_sums = sb("inv_sums", [128, 2, HEADS])
        pt = sb("pt", [128, HEADS, NODES])
        ct_hi = sb("ct_hi", [128, PAIRS, NODES], F32R)
        ct_lo = sb("ct_lo", [128, PAIRS, NODES], F32R)
        y = sb("y", [128, 2, FEAT])

        ps_s = ps("ps_s", [128, 2, 512])
        ps_pt = ps("ps_pt", [128, 2, 512])
        ps_qk = [ps(f"ps_qk{i}", [128, COLS]) for i in range(2)]
        ps_t = ps("ps_t", [128, 512])
        ps_r = ps("ps_r", [128, 512])

        w_loaded = sem("w_loaded")
        w_split = sem("w_split")
        pool_const = sem("pool_const")
        bv_ready = sem("bv_ready")
        ob_ps = sem("ob_ps")
        ob_ready = sem("ob_ready")
        x_loaded = [sem(f"x_loaded{r}") for r in range(RING)]
        adj_loaded = [sem(f"adj_loaded{p}") for p in range(2)]
        bn_done = sem("bn_done")
        moments_ready = sem("moments_ready")
        rstd_step = sem("rstd_step")
        norm_ready = sem("norm_ready")
        h_ready = sem("h_ready")
        ht_ps = sem("ht_ps")
        ht_hi_ready = sem("ht_hi_ready")
        ht_lo_ready = sem("ht_lo_ready")
        qk_ps = sem("qk_ps")
        qk_ready = sem("qk_ready")
        v_ps = sem("v_ps")
        v_ready = sem("v_ready")
        mask_step = sem("mask_step")
        mask_ready = sem("mask_ready")
        scores_ps = sem("scores_ps")
        masked = sem("masked")
        max_ready = sem("max_ready")
        exp_done = sem("exp_done")
        inv_ready = sem("inv_ready")
        probs_ready = sem("probs_ready")
        pt_ps = sem("pt_ps")
        pt_ready = sem("pt_ready")
        ct_ps = sem("ct_ps")
        ct_hi_ready = sem("ct_hi_ready")
        ct_lo_ready = sem("ct_lo_ready")
        proj_ps = sem("proj_ps")
        xb_ready = sem("xb_ready")
        y_ready = sem("y_ready")
        stored = [sem(f"stored{i}") for i in range(2)]

        def valid(u):
            return not isinstance(u, int) or 0 <= u < GRAPHS

        def wait(eng, semaphore, value):
            if not isinstance(value, int) or value > 0:
                eng.wait_ge(semaphore, value)

        def slots(eng, slot):
            for t in range(-LOAD, FIRST):
                slot(t, t % RING)
            with eng.Fori(FIRST, LOOP_END - RING + 1, RING) as base:
                for i in range(RING):
                    slot(base + i, FIRST + i)
            for t in range(LOOP_END, GRAPHS + LATE):
                slot(t, t % RING)

        def turns(u, k, d):
            r = (k + d) % RING
            return 2 * (u - r) + 16

        def group_of(t, k):
            return (k % RING) // GROUP, k % GROUP

        def tiles_of(j):
            return ([0, 1], [2], [3, 4], [5])[j]

        x_rows = x.rearrange("g n f -> n g f")
        out_rows = out.rearrange("g n f -> n g f")
        adj_rows = adj.rearrange("g q k -> q g k")

        block = ctx.enter_context(nc.Block())

        @block.sync
        def _(sp):
            for n, w in zip("qkvf", (Wq, Wk, Wv, Wf)):
                sp.dma_start(w_raw[n][:, :, :], w.rearrange("(k p) n -> p k n", p=128)).then_inc(w_loaded, 16)
            with nc.allow_non_contiguous_dma(reason="three bias vectors, once"):
                for i, b in enumerate((bq, bk)):
                    sp.dma_start(qk_bias[:, i, :], b.rearrange("(k p) -> p k", p=128)).then_inc(w_loaded, 16)
                sp.dma_start(bv_col[:, :], bv.rearrange("(k p) -> p k", p=128)).then_inc(w_loaded, 16)
            sp.dma_start(bf_row[:, :], bf.rearrange("(a n) -> a n", a=1)).then_inc(w_loaded, 16)

            def slot(t, k):
                if valid(t + LOAD):
                    u, r = t + LOAD, (k + LOAD) % RING
                    wait(sp, xb_ready, u - RING + 1)
                    sp.dma_start(x_in[:, r, :], x_rows[:, bass.ds(u, 1), :].rearrange("n g f -> n (g f)")
                                 ).then_inc(x_loaded[r], 16)
                if k % GROUP == 1 and valid(t + 3):
                    if isinstance(t, int):
                        wait(sp, mask_ready, t - 1)
                    sp.dma_start(adj_in[:, ((k + 3) % RING) // GROUP, :, :], adj_rows[:, bass.ds(t + 3, GROUP), :]
                                 ).then_inc(adj_loaded[((k + 3) % RING) // GROUP], 16)
                if valid(t - LATE):
                    u, r = t - LATE, (k - LATE) % 2
                    wait(sp, y_ready, u + 1)
                    sp.dma_start(out_rows[:, bass.ds(u, 1), :].rearrange("n g f -> n (g f)"), y[:, r, :]
                                 ).then_inc(stored[r], 16)

            slots(sp, slot)
            for r in range(2):
                sp.wait_ge(stored[r], 16 * GRAPHS // 2)

        @block.tensor
        def _(pe):
            mm = nc.tensor.matmul

            def split_product(psum, parts_a, parts_b, inc):
                todo = [(a, b, i) for i in range(KT) for a, b in ((0, 0), (0, 1), (1, 0))]
                for n, (a, b, i) in enumerate(todo):
                    last = mm(psum, parts_a[a](i), parts_b[b](i), start=n == 0, stop=n == len(todo) - 1)
                last.then_inc(*inc)

            pe.wait_ge(bv_ready, 1)
            pe.wait_ge(pool_const, 4)
            for i in range(KT):
                mm(ps_r[:, 0:FEAT], bv_wide[:, i, :], w_raw["f"][:, i, :], start=i == 0, stop=False)
            mm(ps_r[:, 0:FEAT], ones[0:1, :], bf_row[:, :], start=False, stop=True).then_inc(ob_ps, 1)
            pe.wait_ge(w_split, 8)
            pe.wait_ge(ob_ready, 1)

            def slot(t, k):
                p, j = group_of(t, k)

                if valid(t):
                    cols = slice(j * NODES, (j + 1) * NODES)
                    if j == 0:
                        wait(pe, qk_ready, 2 * (t + GROUP))
                    wait(pe, masked, 2 * t)
                    for pair in range(PAIRS):
                        for odd in range(2):
                            rows = slice(odd * HEAD, (odd + 1) * HEAD)
                            last = mm(ps_s[:, odd, pair * NODES:(pair + 1) * NODES], qk[rows, p, pair, cols],
                                      qk[rows, p, PAIRS + pair, cols], start=True, stop=True)
                    last.then_inc(scores_ps, 1)

                if valid(t - 1):
                    wait(pe, probs_ready, t)
                    wait(pe, pt_ready, t - 1)
                    for hd in range(HEADS):
                        bank, at = hd // PAIRS, hd % PAIRS
                        last = nc.tensor.transpose(ps_pt[:, bank, at * NODES:(at + 1) * NODES],
                                                   s[:, (k - 1) % 2, hd, :], ident[:, :])
                    last.then_inc(pt_ps, 1)

                g = t - j + GROUP

                def qk_tile(tile):
                    wn, pair = "qk"[tile // PAIRS], tile % PAIRS
                    at = slice(pair * 128, (pair + 1) * 128)
                    n_slot = g - GROUP + j
                    two = len(tiles_of(j)) == 2
                    if two and tile == tiles_of(j)[1]:
                        wait(pe, qk_ready, 2 * (n_slot + GROUP))
                    else:
                        wait(pe, qk_ready, 2 * (n_slot + GROUP) - (1 if not two else 2))
                    split_product(ps_qk[tile % 2][:, :],
                                  [lambda i: w_hi[wn][:, i, at], lambda i: w_lo[wn][:, i, at]],
                                  [lambda i: ht_hi[:, 1 - p, i, :], lambda i: ht_lo[:, 1 - p, i, :]],
                                  (qk_ps, 1 if two else 2))

                if valid(g):
                    if j == 0:
                        wait(pe, ht_hi_ready, g + GROUP)
                        wait(pe, ht_lo_ready, g + GROUP)
                    wait(pe, y_ready, t - 1)
                    if isinstance(t, int):
                        wait(pe, v_ready, t + GROUP)
                    at = slice(j * NODES, (j + 1) * NODES)
                    split_product(ps_r[:, 0:FEAT],
                                  [lambda i: ht_hi[:, 1 - p, i, at], lambda i: ht_lo[:, 1 - p, i, at]],
                                  [lambda i: w_hi["v"][:, i, :], lambda i: w_lo["v"][:, i, :]], (v_ps, 1))

                if valid(t - 1):
                    pp, jj = group_of(t - 1, k - 1 + RING)
                    wait(pe, v_ready, t)
                    wait(pe, pt_ready, t)
                    wait(pe, ht_lo_ready, min(t + 8, GRAPHS) if isinstance(t, int) else t + 8)
                    for pair in range(PAIRS):
                        for odd in range(2):
                            rows = slice(odd * HEAD, (odd + 1) * HEAD)
                            f = (2 * pair + odd) * HEAD
                            last = mm(ps_t[rows, pair * NODES:(pair + 1) * NODES], v[:, pp, jj, f:f + HEAD],
                                      pt[:, odd * PAIRS + pair, :], start=True, stop=True)
                    last.then_inc(ct_ps, 1)

                if valid(g):
                    for tile in tiles_of(j):
                        qk_tile(tile)

                if valid(t + NORM):
                    u = t + NORM
                    wait(pe, h_ready, u + 1)
                    wait(pe, ct_lo_ready, t)
                    if isinstance(t, int):
                        wait(pe, ht_lo_ready, u)
                    for i in range(KT):
                        last = nc.tensor.transpose(ps_t[:, i * 128:(i + 1) * 128],
                                                   h[:, (k + NORM) % 2, i * 128:(i + 1) * 128], ident[:, :])
                    last.then_inc(ht_ps, 1)

                if valid(t - 1):
                    wait(pe, ct_hi_ready, t)
                    wait(pe, ct_lo_ready, t)
                    wait(pe, v_ready, min(t + 5, GRAPHS) if isinstance(t, int) else t + 5)
                    if isinstance(t, int):
                        wait(pe, y_ready, t - 1)
                    split_product(ps_r[:, 0:FEAT], [lambda i: ct_hi[:, i, :], lambda i: ct_lo[:, i, :]],
                                  [lambda i: w_hi["f"][:, i, :], lambda i: w_lo["f"][:, i, :]], (proj_ps, 1))

            slots(pe, slot)

        @block.scalar
        def _(act):
            activation = nc.scalar.activation
            act.wait_ge(w_loaded, 16 * 8)
            for n in "qkvf":
                activation(w_hi[n][:, :, :], w_raw[n][:, :, :], ACT.Copy).then_inc(w_split, 1)

            def slot(t, k):
                p, j = group_of(t, k)

                if valid(t - 1):
                    wait(act, pt_ps, t)
                    wait(act, ct_ps, t - 1)
                    activation(pt[:, :, :].rearrange("p (b h) n -> p b (h n)", b=2), ps_pt[:, :, 0:PAIRS * NODES],
                               ACT.Copy).then_inc(pt_ready, 1)

                if valid(t + NORM):
                    u, r = t + NORM, (k + NORM) % RING
                    wait(act, norm_ready, u + 1)
                    wait(act, x_loaded[r], turns(u, k, NORM))
                    wait(act, ht_ps, u - 1)
                    activation(h[:, r % 2, :], x_in[:, r, :], ACT.Relu, bias=shift[:, r % 2, 1:2],
                               scale=rstd[:, r % 2, 1:2]).then_inc(h_ready, 1)

                if valid(t + GROUP):
                    wait(act, v_ps, t + GROUP + 1)
                    wait(act, ct_ps, t - 3)
                    activation(v[:, 1 - p, j, :], ps_r[:, 0:FEAT], ACT.Copy).then_inc(v_ready, 1)

                if valid(t - 1):
                    wait(act, ct_ps, t)
                    wait(act, proj_ps, t - 1)
                    activation(ct_hi[:, :, :].rearrange("p a n -> p (a n)"), ps_t[:, 0:FEAT],
                               ACT.Copy).then_inc(ct_hi_ready, 1)

                if valid(t):
                    b = k % 2
                    wait(act, max_ready, t + 1)
                    wait(act, inv_ready, t - 1)
                    for hd in range(HEADS):
                        last = activation(s[:, b, hd, :], s[:, b, hd, :], ACT.Exp, bias=neg_max[:, b, hd:hd + 1],
                                          accum_out=sums[:, b, hd:hd + 1])
                    last.then_inc(exp_done, 1)

                if valid(t + NORM):
                    u = t + NORM
                    pu, ju = group_of(u, k + NORM)
                    wait(act, ht_ps, u + 1)
                    if j == 0:
                        wait(act, qk_ps, 2 * (t + GROUP))
                        wait(act, v_ps, t + GROUP)
                    activation(ht_hi[:, pu, :, ju * NODES:(ju + 1) * NODES],
                               ps_t[:, 0:FEAT].rearrange("p (k n) -> p k n", k=KT),
                               ACT.Copy).then_inc(ht_hi_ready, 1)

            slots(act, slot)

        @block.vector
        def _(dve):
            tt = nc.vector.tensor_tensor
            dve.wait_ge(w_loaded, 16 * 8)
            nc.vector.tensor_copy(bv_wide[:, :, :], bv_col[:, :].unsqueeze(2).to_broadcast([128, KT, 128])
                                  ).then_inc(bv_ready, 1)
            for i, n in enumerate("qkvf"):
                dve.wait_ge(w_split, i + 1)
            for n in "qkvf":
                dve.wait_ge(w_split, 4)
                tt(w_lo[n][:, :, :], w_raw[n][:, :, :], w_hi[n][:, :, :].bitcast(F32), ALU.subtract).then_inc(w_split, 1)
            dve.wait_ge(ob_ps, 1)
            nc.vector.tensor_copy(out_bias[:, :], ps_r[:, 0:FEAT]).then_inc(ob_ready, 1)

            def slot(t, k):
                p, j = group_of(t, k)

                if valid(t - LATE):
                    u, r = t - LATE, (k - LATE) % RING
                    wait(dve, proj_ps, u + 1)
                    wait(dve, xb_ready, u + 1)
                    if not isinstance(t, int) or u >= 2:
                        wait(dve, stored[r % 2], 8 * (u - r % 2))
                    tt(y[:, r % 2, :], ps_r[:, 0:FEAT], x_bias[:, r, :], ALU.add).then_inc(y_ready, 1)

                if valid(t):
                    b = k % 2
                    wait(dve, scores_ps, t + 1)
                    wait(dve, mask_ready, t + 1)
                    wait(dve, pt_ps, t - 1)
                    for odd in range(2):
                        nc.vector.scalar_tensor_tensor(
                            out=s[:, b, odd * PAIRS:(odd + 1) * PAIRS, :],
                            in0=ps_s[:, odd, 0:PAIRS * NODES].rearrange("p (h n) -> p h n", h=PAIRS), scalar=SCALE,
                            in1=mask[:, b:b + 1, :].to_broadcast([128, PAIRS, NODES]), op0=ALU.mult, op1=ALU.add,
                        ).then_inc(masked, 1)

                if valid(t + STATS):
                    u, r = t + STATS, (k + STATS) % RING
                    wait(dve, x_loaded[r], turns(u, k, STATS))
                    nc.vector.bn_stats(stats[:, r % 2, :], x_in[:, r, :]).then_inc(bn_done, 1)
                    wait(dve, norm_ready, u - 1)
                    dve.wait_ge(bn_done, u + 1)
                if valid(t):
                    wait(dve, exp_done, t - 1)
                    dve.wait_ge(masked, 2 * t + 2)
                    nc.vector.tensor_reduce(neg_max[:, b, :], s[:, b, :, :], AX.X, ALU.max,
                                            negate=True).then_inc(max_ready, 1)
                if valid(t + STATS):
                    nc.vector.bn_aggr(moments[:, r % 2, :], stats[:, r % 2, :]).then_inc(moments_ready, 1)

                def qk_tile(tile):
                    which, pair = tile // PAIRS, tile % PAIRS
                    two = len(tiles_of(j)) == 2
                    n = 2 * (t + GROUP) + (1 if two and tile == tiles_of(j)[0] else 2)
                    wait(dve, qk_ps, n)
                    if j == 0 and tile == 0:
                        wait(dve, scores_ps, t)
                    nc.vector.tensor_scalar(qk[:, 1 - p, tile, :], ps_qk[tile % 2][:, :],
                                            qk_bias[:, which, pair:pair + 1], None, ALU.add
                                            ).then_inc(qk_ready, 1 if two else 2)

                if valid(t - 1):
                    wait(dve, ct_hi_ready, t)
                    tt(ct_lo[:, :, :].rearrange("p a n -> p (a n)"), ps_t[:, 0:FEAT],
                       ct_hi[:, :, :].rearrange("p a n -> p (a n)").bitcast(F32), ALU.subtract
                       ).then_inc(ct_lo_ready, 1)

                if valid(t + GROUP):
                    qk_tile(tiles_of(j)[0])

                if valid(t):
                    wait(dve, exp_done, t + 1)
                    wait(dve, probs_ready, t - 1)
                    nc.vector.reciprocal(inv_sums[:, k % 2, :], sums[:, k % 2, :]).then_inc(inv_ready, 1)

                if valid(t + GROUP):
                    for tile in tiles_of(j)[1:]:
                        qk_tile(tile)

                if valid(t + NORM):
                    u = t + NORM
                    pu, ju = group_of(u, k + NORM)
                    at = slice(ju * NODES, (ju + 1) * NODES)
                    wait(dve, ht_hi_ready, u + 1)
                    tt(ht_lo[:, pu, :, at], ps_t[:, 0:FEAT].rearrange("p (k n) -> p k n", k=KT),
                       ht_hi[:, pu, :, at].bitcast(F32), ALU.subtract).then_inc(ht_lo_ready, 1)

            slots(dve, slot)

        @block.gpsimd
        def _(pool):
            nc.gpsimd.memset(ident[:, :], 0.0).then_inc(pool_const, 1)
            nc.gpsimd.memset(ones[:, :], 1.0).then_inc(pool_const, 1)
            nc.gpsimd.memset(minus_half[:, :], -0.5).then_inc(pool_const, 1)
            pool.wait_ge(pool_const, 3)
            nc.gpsimd.affine_select(out=ident[:, :], in_=ident[:, :], compare_op=ALU.not_equal, fill=1.0, base=0,
                                    pattern=[[-1, 128]], channel_multiplier=1).then_inc(pool_const, 1)
            pool.wait_ge(pool_const, 4)
            pool.wait_ge(ob_ready, 1)

            def slot(t, k):
                if valid(t + XB):
                    wait(pool, h_ready, t + XB + 1)
                    wait(pool, y_ready, t - 1)
                if valid(t + STATS):
                    wait(pool, moments_ready, t + STATS + 1)
                    wait(pool, h_ready, t + STATS - 1)
                if valid(t + 1):
                    pu, ju = group_of(t + 1, k + 1)
                    if ju == 0:
                        wait(pool, adj_loaded[pu], 2 * (t + 1 - pu * GROUP) + 16)
                    wait(pool, masked, 2 * t)

                if valid(t + XB):
                    r = (k + XB) % RING
                    nc.gpsimd.tensor_tensor(x_bias[:, r, :], x_in[:, r, :], out_bias[:, :], ALU.add
                                            ).then_inc(xb_ready, 1)

                if valid(t + STATS):
                    u, b = t + STATS, (k + STATS) % 2
                    nc.gpsimd.tensor_scalar(rstd[:, b, 0:1], moments[:, b, 1:2], EPS, None, ALU.add
                                            ).then_inc(rstd_step, 1)
                    nc.gpsimd.tensor_scalar(shift[:, b, 0:1], moments[:, b, 0:1], -1.0, None, ALU.mult
                                            ).then_inc(rstd_step, 1)

                if valid(t + 1):
                    nc.gpsimd.tensor_scalar(mask[:, (k + 1) % 2, :], adj_in[:, pu, ju, :], -NEG, NEG,
                                            ALU.mult, ALU.add).then_inc(mask_ready, 1)

                if valid(t + STATS):
                    pool.wait_ge(rstd_step, 3 * u + 2)
                    nc.gpsimd.tensor_tensor(rstd[:, b, 1:2], rstd[:, b, 0:1], minus_half[:, :], ALU.pow
                                            ).then_inc(rstd_step, 1)
                    pool.wait_ge(rstd_step, 3 * u + 3)
                    nc.gpsimd.tensor_tensor(shift[:, b, 1:2], shift[:, b, 0:1], rstd[:, b, 1:2], ALU.mult
                                            ).then_inc(norm_ready, 1)

                if valid(t):
                    b = k % 2
                    wait(pool, inv_ready, t + 1)
                    nc.gpsimd.tensor_tensor(s[:, b, :, :], s[:, b, :, :],
                                            inv_sums[:, b, :].unsqueeze(2).to_broadcast([128, HEADS, NODES]),
                                            ALU.mult).then_inc(probs_ready, 1)

            slots(pool, slot)


_INS = ["x", "adj"] + [f"L0_gnn_{n}" for n in ("Wq", "bq", "Wk", "bk", "Wv", "bv", "Wf", "bf")]


def kernel(**inputs):
    import numpy as _np
    import concourse.bacc as _bacc
    from concourse import mybir as _mybir
    from concourse.bass_utils import run_bass_kernel_spmd as _run

    nc = _bacc.Bacc("TRN2", target_bir_lowering=False, num_devices=1)
    arrays, args = {}, []
    for name in _INS:
        a = _np.ascontiguousarray(inputs[name])
        arrays[f"in_{name}"] = a
        args.append(nc.dram_tensor(f"in_{name}", a.shape, _mybir.dt.from_np(a.dtype), kind="ExternalInput").ap())
    shape = inputs["x"].shape
    args.append(nc.dram_tensor("out_0", shape, _mybir.dt.float32, kind="ExternalOutput").ap())
    graph_attention(nc, *args)
    r = _run(nc, [arrays], core_ids=[0])
    return r.results[0]["out_0"]
```

```python
from contextlib import ExitStack

import concourse.bass as bass
from concourse import mybir

F32 = mybir.dt.float32
F32R = mybir.dt.float32r
F16 = mybir.dt.float16
I32 = mybir.dt.int32
U8 = mybir.dt.uint8
ALU = mybir.AluOpType
ACT = mybir.ActivationFunctionType
AX = mybir.AxisListType

GRAPHS, NODES, FEAT = 128, 128, 384
HEADS, HEAD = 6, 64
PAIRS = HEADS // 2
KT = FEAT // 128
GROUP = 4
COLS = GROUP * NODES
TILES = 2 * PAIRS
RING = 2 * GROUP
NEG = -9000000000000000.0
EPS = 1e-5
SCALE = 1.0 / HEAD ** 0.5

LOAD, STATS, NORM, LATE = 12, 9, 8, 2
XB = 3
EXPONENT = 0x7F800000
TOP = 16.0
TINY = 2.0 ** -100
FIRST, LOOP_END = 4, GRAPHS - 12


def graph_attention(nc, x, adj, Wq, bq, Wk, bk, Wv, bv, Wf, bf, out):
    ctx = ExitStack()
    with ctx:
        def sb(name, shape, dt=F32):
            return ctx.enter_context(nc.sbuf_tensor(name, shape, dt))

        def ps(name, shape):
            return ctx.enter_context(nc.psum_tensor(name, shape, F32))

        def sem(name):
            return ctx.enter_context(nc.semaphore(name))

        w_raw = {n: sb(f"w_raw_{n}", [128, KT, FEAT]) for n in "qkvf"}
        w_hi = {n: sb(f"w_hi_{n}", [128, KT, FEAT], F32R) for n in "qkvf"}
        w_lo = {n: sb(f"w_lo_{n}", [128, KT, FEAT], F32R) for n in "qkvf"}
        qk_bias = sb("qk_bias", [128, 2, PAIRS])
        bv_col = sb("bv_col", [128, KT])
        bv_wide = sb("bv_wide", [128, KT, 128])
        bf_row = sb("bf_row", [1, FEAT])
        out_bias = sb("out_bias", [128, FEAT])
        largest = sb("largest", [128, 2, 3])
        largest_all = sb("largest_all", [128, 2])
        power = sb("power", [128, 2])
        w_scale = sb("w_scale", [128, 2])
        unscale = sb("unscale", [128, 3])
        ident = sb("ident", [128, 128])
        ones = sb("ones", [128, 128])
        minus_half = sb("minus_half", [128, 1])
        x_in = sb("x_in", [128, RING, FEAT])
        x_bias = sb("x_bias", [128, RING, FEAT])
        adj_in = sb("adj_in", [128, 2, GROUP, NODES], U8)
        mask = sb("mask", [128, 2, NODES])
        stats = sb("stats", [128, 2, 6])
        moments = sb("moments", [128, 2, 2])
        rstd = sb("rstd", [128, 2, 2])
        shift = sb("shift", [128, 2, 2])
        h = sb("h", [128, 2, FEAT])
        ht_hi = sb("ht_hi", [128, 2, KT, COLS], F32R)
        ht_lo = sb("ht_lo", [128, 2, KT, COLS], F32R)
        q_st = sb("q_st", [128, 2, PAIRS, 2, COLS], F16)
        k_hi = sb("k_hi", [128, 2, PAIRS, 2, COLS], F16)
        k_lo = sb("k_lo", [128, 2, PAIRS, 2, COLS], F16)
        q_low = sb("q_low", [128, 2, COLS], F16)
        v = sb("v", [128, 2, GROUP, FEAT])
        s = sb("s", [128, 2, HEADS, NODES])
        neg_max = sb("neg_max", [128, 2, HEADS])
        sums = sb("sums", [128, 2, HEADS])
        inv_sums = sb("inv_sums", [128, 2, HEADS])
        pt = sb("pt", [128, HEADS, NODES])
        ct_hi = sb("ct_hi", [128, PAIRS, NODES], F32R)
        ct_lo = sb("ct_lo", [128, PAIRS, NODES], F32R)
        y = sb("y", [128, 2, FEAT])

        ps_s = ps("ps_s", [128, 2, 512])
        ps_pt = ps("ps_pt", [128, 2, 512])
        ps_qk = [ps(f"ps_qk{i}", [128, COLS]) for i in range(2)]
        ps_t = ps("ps_t", [128, 512])
        ps_r = ps("ps_r", [128, 512])

        w_loaded = {n: sem(f"w_loaded_{n}") for n in "qkvf"}
        qk_bias_loaded = sem("qk_bias_loaded")
        vf_bias_loaded = sem("vf_bias_loaded")
        w_hi_ready = sem("w_hi_ready")
        w_lo_ready = sem("w_lo_ready")
        scale_step = sem("scale_step")
        largest_ready = sem("largest_ready")
        scale_ready = sem("scale_ready")
        pool_const = sem("pool_const")
        bv_ready = sem("bv_ready")
        ob_ps = sem("ob_ps")
        ob_ready = sem("ob_ready")
        x_loaded = [sem(f"x_loaded{r}") for r in range(RING)]
        adj_loaded = [sem(f"adj_loaded{p}") for p in range(2)]
        bn_done = sem("bn_done")
        moments_ready = sem("moments_ready")
        rstd_step = sem("rstd_step")
        norm_ready = sem("norm_ready")
        h_ready = sem("h_ready")
        ht_ps = sem("ht_ps")
        ht_hi_ready = sem("ht_hi_ready")
        ht_lo_ready = sem("ht_lo_ready")
        qk_ps = sem("qk_ps")
        qk_hi_ready = sem("qk_hi_ready")
        qk_out = sem("qk_out")
        odd_moved = sem("odd_moved")
        qk_ready = sem("qk_ready")
        v_ps = sem("v_ps")
        v_ready = sem("v_ready")
        mask_step = sem("mask_step")
        mask_ready = sem("mask_ready")
        scores_ps = sem("scores_ps")
        masked = sem("masked")
        max_ready = sem("max_ready")
        exp_done = sem("exp_done")
        inv_ready = sem("inv_ready")
        probs_ready = sem("probs_ready")
        pt_ps = sem("pt_ps")
        pt_ready = sem("pt_ready")
        ct_ps = sem("ct_ps")
        ct_hi_ready = sem("ct_hi_ready")
        ct_lo_ready = sem("ct_lo_ready")
        proj_ps = sem("proj_ps")
        xb_ready = sem("xb_ready")
        y_ready = sem("y_ready")
        stored = [sem(f"stored{i}") for i in range(2)]

        def valid(u):
            return not isinstance(u, int) or 0 <= u < GRAPHS

        def wait(eng, semaphore, value):
            if not isinstance(value, int) or value > 0:
                eng.wait_ge(semaphore, value)

        def slots(eng, slot, weights=lambda t: None):
            for t in range(-LOAD, FIRST):
                weights(t)
                slot(t, t % RING)
            with eng.Fori(FIRST, LOOP_END - RING + 1, RING) as base:
                for i in range(RING):
                    slot(base + i, FIRST + i)
            for t in range(LOOP_END, GRAPHS + LATE):
                slot(t, t % RING)

        def turns(u, k, d):
            r = (k + d) % RING
            return 2 * (u - r) + 16

        def group_of(t, k):
            return (k % RING) // GROUP, k % GROUP

        TILE = [(0, 0), (1, 0), (1, 1), (0, 1), (1, 2), (0, 2)]
        PROJECTED = [[0, 1], [2], [3, 4], [5]]
        STACKED = [0, 1, 2, 3, 5, 4]
        COUNT = [1, 1, 2, 1, 1, 2]

        def stacked_to(tile):
            return sum(COUNT[:STACKED.index(tile) + 1])

        def stack_count(t, j, tile):
            return 2 * (t - j + GROUP) + stacked_to(tile)

        def tile_count(t, j, tile):
            slot = next(i for i in range(GROUP) if tile in PROJECTED[i])
            return 2 * (t + GROUP) + 2 * (slot - j) + (1 if PROJECTED[slot][-1] != tile else 2)

        x_rows = x.rearrange("g n f -> n g f")
        out_rows = out.rearrange("g n f -> n g f")
        adj_rows = adj.rearrange("g q k -> q g k")

        block = ctx.enter_context(nc.Block())

        @block.sync
        def _(sp):
            def load_weight(n, w):
                sp.dma_start(w_raw[n][:, :, :], w.rearrange("(k p) n -> p k n", p=128)).then_inc(w_loaded[n], 16)

            def weights(t):
                column = lambda b: b.rearrange("(k p) -> p k", p=128)
                if t == 2 - LOAD:
                    load_weight("q", Wq)
                if t == 4 - LOAD:
                    load_weight("k", Wk)
                    with nc.allow_non_contiguous_dma(reason="bias vectors, once"):
                        for i, b in enumerate((bq, bk)):
                            sp.dma_start(qk_bias[:, i, :], column(b)).then_inc(qk_bias_loaded, 16)
                    load_weight("v", Wv)
                if t == 5 - LOAD:
                    with nc.allow_non_contiguous_dma(reason="a bias vector, once"):
                        sp.dma_start(bv_col[:, :], column(bv)).then_inc(vf_bias_loaded, 16)
                    sp.dma_start(bf_row[:, :], bf.rearrange("(a n) -> a n", a=1)).then_inc(vf_bias_loaded, 16)
                    load_weight("f", Wf)

            def slot(t, k):
                if valid(t - LATE):
                    u, r = t - LATE, (k - LATE) % 2
                    wait(sp, y_ready, u + 1)
                    sp.dma_start(out_rows[:, bass.ds(u, 1), :].rearrange("n g f -> n (g f)"), y[:, r, :]
                                 ).then_inc(stored[r], 16)
                if valid(t + LOAD):
                    u, r = t + LOAD, (k + LOAD) % RING
                    wait(sp, xb_ready, u - RING + 1)
                    sp.dma_start(x_in[:, r, :], x_rows[:, bass.ds(u, 1), :].rearrange("n g f -> n (g f)")
                                 ).then_inc(x_loaded[r], 16)
                if k % GROUP == 0 and valid(t + GROUP):
                    at = (k % RING) // GROUP ^ 1
                    if isinstance(t, int):
                        wait(sp, mask_ready, t)
                    sp.dma_start(adj_in[:, at, :, :], adj_rows[:, bass.ds(t + GROUP, GROUP), :]
                                 ).then_inc(adj_loaded[at], 16)

            slots(sp, slot, weights)
            for r in range(2):
                sp.wait_ge(stored[r], 16 * GRAPHS // 2)

        @block.tensor
        def _(pe):
            mm = nc.tensor.matmul

            def split_product(psum, parts_a, parts_b, inc):
                todo = [(a, b, i) for i in range(KT) for a, b in ((0, 0), (0, 1), (1, 0))]
                for n, (a, b, i) in enumerate(todo):
                    last = mm(psum, parts_a[a](i), parts_b[b](i), start=n == 0, stop=n == len(todo) - 1)
                last.then_inc(*inc)

            def output_bias():
                pe.wait_ge(bv_ready, 1)
                pe.wait_ge(w_loaded["f"], 16)
                pe.wait_ge(vf_bias_loaded, 32)
                for i in range(KT):
                    mm(ps_s[:, 0, 0:FEAT], bv_wide[:, i, :], w_raw["f"][:, i, :], start=i == 0, stop=False)
                mm(ps_s[:, 0, 0:FEAT], ones[0:1, :], bf_row[:, :], start=False, stop=True).then_inc(ob_ps, 1)

            pe.wait_ge(pool_const, 4)

            def slot(t, k):
                p, j = group_of(t, k)
                tiles = PROJECTED[j]
                two = len(tiles) == 2
                done = t + GROUP
                project = valid(done)
                last_slots = isinstance(t, int) and t >= GRAPHS - GROUP
                start = isinstance(t, int) and t == -GROUP

                def scores(t, k):
                    if not valid(t):
                        return
                    p, j = group_of(t, k)
                    cols = slice(j * NODES, (j + 1) * NODES)
                    wait(pe, masked, 2 * t)
                    if isinstance(t, int) and t == 0:
                        wait(pe, ob_ready, 1)
                    for pair in range(PAIRS):
                        if j == 0:
                            wait(pe, qk_ready, 2 * t + max(stacked_to(i) for i in range(TILES) if TILE[i][1] == pair))
                        for odd in range(2):
                            for part in (k_hi, k_lo):
                                last = mm(ps_s[:, odd, pair * NODES:(pair + 1) * NODES], q_st[:, p, pair, odd, cols],
                                          part[:, p, pair, odd, cols], start=part is k_hi, stop=part is k_lo)
                    last.then_inc(scores_ps, 1)

                def projection():
                    if not valid(t - 1):
                        return
                    wait(pe, ct_hi_ready, t)
                    wait(pe, ct_lo_ready, t)
                    if isinstance(t, int) and t == 1:
                        wait(pe, w_hi_ready, 4)
                        wait(pe, w_lo_ready, 4)
                    if two and project:
                        wait(pe, v_ready, done + 1)
                    else:
                        wait(pe, y_ready, t - 1)
                    split_product(ps_r[:, 0:FEAT], [lambda i: ct_hi[:, i, :], lambda i: ct_lo[:, i, :]],
                                  [lambda i: w_hi["f"][:, i, :], lambda i: w_lo["f"][:, i, :]], (proj_ps, 1))

                def transposed_probs(odd):
                    if not valid(t - 1):
                        return
                    if odd == 0:
                        wait(pe, pt_ready, t - 1)
                    wait(pe, probs_ready, 2 * t - 1 + odd)
                    for pair in range(PAIRS):
                        last = nc.tensor.transpose(ps_pt[:, odd, pair * NODES:(pair + 1) * NODES],
                                                   s[:, (k - 1) % 2, odd * PAIRS + pair, :], ident[:, :])
                    if odd == 1:
                        last.then_inc(pt_ps, 1)

                def qk_tile(tile):
                    if not project:
                        return
                    wn, pair = "qk"[TILE[tile][0]], TILE[tile][1]
                    at = slice(pair * 128, (pair + 1) * 128)
                    if start:
                        wait(pe, w_hi_ready, 2 + tile)
                        wait(pe, w_lo_ready, 2 + tile)
                    if j == 0 and tile == tiles[0]:
                        wait(pe, ht_hi_ready, done + GROUP)
                        wait(pe, ht_lo_ready, done + GROUP)
                    if two and tile == tiles[0]:
                        wait(pe, v_ready, done)
                    else:
                        wait(pe, qk_out, 2 * done - (0 if two else 1))
                    split_product(ps_qk[tile % 2][:, :],
                                  [lambda i: w_hi[wn][:, i, at], lambda i: w_lo[wn][:, i, at]],
                                  [lambda i: ht_hi[:, 1 - p, i, :], lambda i: ht_lo[:, 1 - p, i, :]],
                                  (qk_ps, 1 if two else 2))

                def v_tile():
                    if not project:
                        return
                    if start:
                        wait(pe, w_hi_ready, 1)
                        wait(pe, w_lo_ready, 1)
                        wait(pe, ht_hi_ready, 1)
                        wait(pe, ht_lo_ready, 1)
                    if two:
                        wait(pe, y_ready, t - 1)
                        if isinstance(t, int):
                            wait(pe, v_ready, done)
                        psum = ps_r[:, 0:FEAT]
                    else:
                        wait(pe, qk_out, 2 * done)
                        psum = ps_qk[1 - tiles[0] % 2][:, 0:FEAT]
                    at = slice(j * NODES, (j + 1) * NODES)
                    split_product(psum, [lambda i: ht_hi[:, 1 - p, i, at], lambda i: ht_lo[:, 1 - p, i, at]],
                                  [lambda i: w_hi["v"][:, i, :], lambda i: w_lo["v"][:, i, :]], (v_ps, 1))

                def context():
                    if not valid(t - 1):
                        return
                    pp, jj = group_of(t - 1, k - 1 + RING)
                    wait(pe, v_ready, t)
                    wait(pe, pt_ready, t)
                    wait(pe, ht_lo_ready, min(t + NORM, GRAPHS) if isinstance(t, int) else t + NORM)
                    for pair in range(PAIRS):
                        for odd in range(2):
                            rows = slice(odd * HEAD, (odd + 1) * HEAD)
                            f = (2 * pair + odd) * HEAD
                            last = mm(ps_t[rows, pair * NODES:(pair + 1) * NODES], v[:, pp, jj, f:f + HEAD],
                                      pt[:, odd * PAIRS + pair, :], start=True, stop=True)
                    last.then_inc(ct_ps, 1)

                def transposed_h():
                    u = t + NORM
                    if not valid(u):
                        return
                    wait(pe, h_ready, u + 1)
                    wait(pe, ct_lo_ready, t)
                    if isinstance(t, int):
                        wait(pe, ht_lo_ready, u)
                    for i in range(KT):
                        last = nc.tensor.transpose(ps_t[:, i * 128:(i + 1) * 128],
                                                   h[:, (k + NORM) % 2, i * 128:(i + 1) * 128], ident[:, :])
                    last.then_inc(ht_ps, 1)

                if last_slots:
                    if t == GRAPHS - GROUP:
                        scores(t, k)
                    transposed_probs(0)
                    transposed_probs(1)
                    scores(t + 1, k + 1)
                    context()
                    projection()
                elif j == 0:
                    scores(t, k)
                    transposed_probs(0)
                    transposed_probs(1)
                    v_tile()
                    context()
                    if start:
                        output_bias()
                    qk_tile(0)
                    transposed_h()
                    qk_tile(1)
                    projection()
                elif j == 1:
                    transposed_probs(0)
                    scores(t, k)
                    transposed_probs(1)
                    qk_tile(2)
                    context()
                    v_tile()
                    projection()
                    transposed_h()
                elif j == 2:
                    scores(t, k)
                    transposed_probs(0)
                    transposed_probs(1)
                    v_tile()
                    context()
                    qk_tile(3)
                    qk_tile(4)
                    transposed_h()
                    projection()
                elif j == 3:
                    scores(t, k)
                    transposed_probs(0)
                    transposed_probs(1)
                    qk_tile(5)
                    context()
                    v_tile()
                    transposed_h()
                    projection()

            slots(pe, slot)

        @block.scalar
        def _(act):
            activation = nc.scalar.activation

            def upper_weights(names):
                for n in names:
                    act.wait_ge(w_loaded[n], 16)
                    if n in "qk":
                        act.wait_ge(scale_ready, 1)
                    scale = w_scale[:, "qk".index(n):"qk".index(n) + 1] if n in "qk" else 1.0
                    activation(w_hi[n][:, :, :], w_raw[n][:, :, :], ACT.Copy, scale=scale).then_inc(w_hi_ready, 1)

            def weights(t):
                if t == -4:
                    upper_weights("qk")
                if t == -3:
                    upper_weights("f")

            def slot(t, k):
                p, j = group_of(t, k)
                tiles = PROJECTED[j]
                two = len(tiles) == 2
                project = valid(t + GROUP)

                def qk_tile(tile):
                    if not project:
                        return
                    which, pair = TILE[tile]
                    wait(act, qk_ps, tile_count(t, j, tile))
                    if j == 0 and tile == 0:
                        wait(act, scores_ps, t)
                    activation((q_st, k_hi)[which][:, 1 - p, pair, 0, :], ps_qk[tile % 2][:, :], ACT.Identity,
                               bias=qk_bias[:, which, pair:pair + 1]).then_inc(qk_hi_ready, 1 if two else 2)

                def v_tile():
                    if not project:
                        return
                    wait(act, v_ps, t + GROUP + 1)
                    wait(act, ct_ps, t - 3)
                    psum = ps_r if two else ps_qk[1 - tiles[0] % 2]
                    activation(v[:, 1 - p, j, :], psum[:, 0:FEAT], ACT.Copy).then_inc(v_ready, 1)

                def exponentials(odd):
                    if not valid(t):
                        return
                    b = k % 2
                    if odd == 0:
                        wait(act, max_ready, t + 1)
                        wait(act, inv_ready, 2 * (t - 1))
                    for hd in range(odd * PAIRS, (odd + 1) * PAIRS):
                        last = activation(s[:, b, hd, :], s[:, b, hd, :], ACT.Exp, bias=neg_max[:, b, hd:hd + 1],
                                          accum_out=sums[:, b, hd:hd + 1])
                    last.then_inc(exp_done, 1)

                def context():
                    if not valid(t - 1):
                        return
                    wait(act, ct_ps, t)
                    wait(act, proj_ps, t - 1)
                    activation(ct_hi[:, :, :].rearrange("p a n -> p (a n)"), ps_t[:, 0:FEAT],
                               ACT.Copy).then_inc(ct_hi_ready, 1)

                def transposed_probs():
                    if not valid(t - 1):
                        return
                    wait(act, pt_ps, t)
                    wait(act, ct_ps, t - 1)
                    activation(pt[:, :, :].rearrange("p (b h) n -> p b (h n)", b=2), ps_pt[:, :, 0:PAIRS * NODES],
                               ACT.Copy).then_inc(pt_ready, 1)

                def norm():
                    u, r = t + NORM, (k + NORM) % RING
                    if not valid(u):
                        return
                    wait(act, norm_ready, u + 1)
                    wait(act, x_loaded[r], turns(u, k, NORM))
                    wait(act, ht_ps, u - 1)
                    activation(h[:, r % 2, :], x_in[:, r, :], ACT.Relu, bias=shift[:, r % 2, 1:2],
                               scale=rstd[:, r % 2, 1:2]).then_inc(h_ready, 1)

                def upper_h():
                    u = t + NORM
                    if not valid(u):
                        return
                    pu, ju = group_of(u, k + NORM)
                    wait(act, ht_ps, u + 1)
                    if j == 0:
                        wait(act, qk_ps, 2 * (t + GROUP))
                        wait(act, v_ps, t + GROUP)
                    activation(ht_hi[:, pu, :, ju * NODES:(ju + 1) * NODES],
                               ps_t[:, 0:FEAT].rearrange("p (k n) -> p k n", k=KT),
                               ACT.Copy).then_inc(ht_hi_ready, 1)

                if isinstance(t, int) and t < -GROUP:
                    norm()
                    if t == -6:
                        upper_weights("v")
                    upper_h()
                elif isinstance(t, int) and t >= GRAPHS - GROUP:
                    transposed_probs()
                    exponentials(0)
                    context()
                    exponentials(1)
                elif j == 0:
                    transposed_probs()
                    norm()
                    v_tile()
                    context()
                    exponentials(0)
                    exponentials(1)
                    qk_tile(0)
                    qk_tile(1)
                    upper_h()
                elif j == 1:
                    transposed_probs()
                    norm()
                    qk_tile(2)
                    context()
                    exponentials(0)
                    exponentials(1)
                    v_tile()
                    upper_h()
                elif j == 2:
                    norm()
                    transposed_probs()
                    v_tile()
                    context()
                    exponentials(0)
                    exponentials(1)
                    qk_tile(3)
                    qk_tile(4)
                    upper_h()
                elif j == 3:
                    transposed_probs()
                    norm()
                    qk_tile(5)
                    context()
                    exponentials(0)
                    exponentials(1)
                    upper_h()
                    v_tile()

            slots(act, slot, weights)

        @block.vector
        def _(dve):
            tt = nc.vector.tensor_tensor
            scalar = nc.vector.tensor_scalar
            copy = nc.vector.tensor_copy
            top, bottom = slice(0, HEAD), slice(HEAD, 2 * HEAD)

            def low_weights(names):
                for n in names:
                    dve.wait_ge(w_hi_ready, "vqkf".index(n) + 1)
                    scale = w_scale[:, "qk".index(n):"qk".index(n) + 1] if n in "qk" else 1.0
                    nc.vector.scalar_tensor_tensor(out=w_lo[n][:, :, :], in0=w_raw[n][:, :, :], scalar=scale,
                                                   in1=w_hi[n][:, :, :].bitcast(F32), op0=ALU.mult, op1=ALU.subtract
                                                   ).then_inc(w_lo_ready, 1)

            def largest_of(i):
                n = "qk"[i]
                dve.wait_ge(w_loaded[n], 16)
                nc.vector.tensor_reduce(largest[:, i, 0:1], w_raw[n][:, :, :], AX.XY, ALU.max,
                                        apply_absolute_value=True).then_inc(scale_step, 1)

            def scales():
                dve.wait_ge(largest_ready, 1)
                scalar(largest[:, :, 2], largest_all[:, :], TINY, None, ALU.max).then_inc(scale_step, 1)
                dve.wait_ge(scale_step, 5)
                scalar(power[:, :].bitcast(I32), largest[:, :, 2].bitcast(I32), EXPONENT, None, ALU.bitwise_and
                       ).then_inc(scale_step, 1)
                dve.wait_ge(scale_step, 6)
                nc.vector.reciprocal(w_scale[:, :], power[:, :]).then_inc(scale_step, 1)
                scalar(unscale[:, 0:2], power[:, :], 1.0 / TOP, None, ALU.mult).then_inc(scale_step, 1)
                dve.wait_ge(scale_step, 8)
                scalar(w_scale[:, :], w_scale[:, :], TOP, None, ALU.mult).then_inc(scale_step, 1)
                scalar(unscale[:, 2:3], unscale[:, 0:1], unscale[:, 1:2], SCALE, ALU.mult, ALU.mult
                       ).then_inc(scale_step, 1)
                dve.wait_ge(scale_step, 10)
                tt(qk_bias[:, :, :], qk_bias[:, :, :], w_scale[:, :].unsqueeze(2).to_broadcast([128, 2, PAIRS]),
                   ALU.mult).then_inc(scale_ready, 1)

            def weights(t):
                if t == -7:
                    largest_of(0)
                if t == -6:
                    largest_of(1)
                    dve.wait_ge(qk_bias_loaded, 32)
                    nc.vector.tensor_reduce(largest[:, :, 1], qk_bias[:, :, :], AX.X, ALU.max,
                                            apply_absolute_value=True).then_inc(scale_step, 1)
                    dve.wait_ge(scale_step, 3)
                    tt(largest[:, :, 2], largest[:, :, 0], largest[:, :, 1], ALU.max).then_inc(scale_step, 1)
                if t == -4:
                    low_weights("v")
                if t == -2:
                    low_weights("f")

            def slot(t, k):
                p, j = group_of(t, k)
                project = valid(t + GROUP)

                def residual():
                    u, r = t - LATE, (k - LATE) % RING
                    if not valid(u):
                        return
                    wait(dve, proj_ps, u + 1)
                    wait(dve, xb_ready, u + 1)
                    if not isinstance(t, int) or u >= 2:
                        wait(dve, stored[r % 2], 8 * (u - r % 2))
                    tt(y[:, r % 2, :], ps_r[:, 0:FEAT], x_bias[:, r, :], ALU.add).then_inc(y_ready, 1)

                def qk_lower(tile):
                    if not project:
                        return
                    which, pair = TILE[tile]
                    wait(dve, qk_hi_ready, tile_count(t, j, tile))
                    upper = (q_st, k_hi)[which][:, 1 - p, pair, 0, :]
                    lower = q_low[:, pair % 2, :] if which == 0 else k_lo[:, 1 - p, pair, 0, :]
                    nc.vector.scalar_tensor_tensor(out=lower, in0=ps_qk[tile % 2][:, :],
                                                   scalar=qk_bias[:, which, pair:pair + 1], in1=upper,
                                                   op0=ALU.add, op1=ALU.subtract).then_inc(qk_out, COUNT[tile])

                def stack_odd(tile):
                    if not project:
                        return
                    which, pair = TILE[tile]
                    dve.wait_ge(qk_out, tile_count(t, j, tile))
                    if which == 0:
                        q = q_st[:, 1 - p, pair, :, :]
                        copy(q[top, 1, :], q_low[bottom, pair % 2, :])
                        last = copy(q[bottom, 1, :], q[bottom, 0, :])
                    else:
                        hi, lo = k_hi[:, 1 - p, pair, :, :], k_lo[:, 1 - p, pair, :, :]
                        copy(hi[bottom, 1, :], hi[bottom, 0, :])
                        copy(hi[top, 1, :], hi[bottom, 0, :])
                        copy(lo[bottom, 1, :], lo[bottom, 0, :])
                        last = copy(lo[top, 1, :], lo[bottom, 0, :])
                    last.then_inc(odd_moved, COUNT[STACKED.index(tile)])

                def stack_even(tile):
                    if not project:
                        return
                    which, pair = TILE[tile]
                    dve.wait_ge(odd_moved, stack_count(t, j, tile))
                    if which == 0:
                        last = copy(q_st[bottom, 1 - p, pair, 0, :], q_low[top, pair % 2, :])
                    else:
                        hi, lo = k_hi[:, 1 - p, pair, 0, :], k_lo[:, 1 - p, pair, 0, :]
                        copy(hi[bottom, :], hi[top, :])
                        last = copy(lo[bottom, :], lo[top, :])
                    last.then_inc(qk_ready, COUNT[STACKED.index(tile)])

                def reciprocals(odd):
                    if not valid(t):
                        return
                    half = slice(odd * PAIRS, (odd + 1) * PAIRS)
                    wait(dve, exp_done, 2 * t + 1 + odd)
                    if odd == 0:
                        wait(dve, probs_ready, 2 * (t - 1))
                    nc.vector.reciprocal(inv_sums[:, k % 2, half], sums[:, k % 2, half]).then_inc(inv_ready, 1)

                def masked_scores(t, k):
                    if not valid(t):
                        return
                    b = k % 2
                    wait(dve, scores_ps, t + 1)
                    wait(dve, mask_ready, t + 1)
                    wait(dve, pt_ps, t - 1)
                    for odd in range(2):
                        nc.vector.scalar_tensor_tensor(
                            out=s[:, b, odd * PAIRS:(odd + 1) * PAIRS, :],
                            in0=ps_s[:, odd, 0:PAIRS * NODES].rearrange("p (h n) -> p h n", h=PAIRS),
                            scalar=unscale[:, 2:3],
                            in1=mask[:, b:b + 1, :].to_broadcast([128, PAIRS, NODES]), op0=ALU.mult, op1=ALU.add,
                        ).then_inc(masked, 1)

                def statistics(t, k):
                    b = k % 2
                    if valid(t + STATS):
                        u, r = t + STATS, (k + STATS) % RING
                        wait(dve, x_loaded[r], turns(u, k, STATS))
                        nc.vector.bn_stats(stats[:, r % 2, :], x_in[:, r, :]).then_inc(bn_done, 1)
                        wait(dve, norm_ready, u - 1)
                        dve.wait_ge(bn_done, u + 1)
                    if valid(t):
                        wait(dve, exp_done, 2 * (t - 1))
                        dve.wait_ge(masked, 2 * t + 2)
                        nc.vector.tensor_reduce(neg_max[:, b, :], s[:, b, :, :], AX.X, ALU.max,
                                                negate=True).then_inc(max_ready, 1)
                    if valid(t + STATS):
                        nc.vector.bn_aggr(moments[:, r % 2, :], stats[:, r % 2, :]).then_inc(moments_ready, 1)

                def lower_context():
                    if not valid(t - 1):
                        return
                    wait(dve, ct_hi_ready, t)
                    tt(ct_lo[:, :, :].rearrange("p a n -> p (a n)"), ps_t[:, 0:FEAT],
                       ct_hi[:, :, :].rearrange("p a n -> p (a n)").bitcast(F32), ALU.subtract
                       ).then_inc(ct_lo_ready, 1)

                def lower_h(ahead):
                    u = t + ahead
                    if not valid(u):
                        return
                    pu, ju = group_of(u, k + ahead + RING)
                    at = slice(ju * NODES, (ju + 1) * NODES)
                    wait(dve, ht_hi_ready, u + 1)
                    tt(ht_lo[:, pu, :, at], ps_t[:, 0:FEAT].rearrange("p (k n) -> p k n", k=KT),
                       ht_hi[:, pu, :, at].bitcast(F32), ALU.subtract).then_inc(ht_lo_ready, 1)

                if isinstance(t, int) and t < -GROUP:
                    statistics(t, k)
                    lower_h(NORM - 1)
                elif isinstance(t, int) and t >= GRAPHS - GROUP:
                    if t == GRAPHS - GROUP:
                        masked_scores(t, k)
                        statistics(t, k)
                    reciprocals(0)
                    residual()
                    lower_context()
                    masked_scores(t + 1, k + 1)
                    reciprocals(1)
                    statistics(t + 1, k + 1)
                elif j == 0:
                    if isinstance(t, int) and t == -GROUP:
                        lower_h(NORM - 1)
                        scales()
                        low_weights("qk")
                    residual()
                    masked_scores(t, k)
                    statistics(t, k)
                    lower_context()
                    reciprocals(0)
                    qk_lower(0)
                    reciprocals(1)
                    stack_odd(0)
                    stack_even(0)
                    qk_lower(1)
                    lower_h(NORM)
                    if isinstance(t, int) and t == -GROUP:
                        dve.wait_ge(ob_ps, 1)
                        copy(out_bias[:, :], ps_s[:, 0, 0:FEAT]).then_inc(ob_ready, 1)
                elif j == 1:
                    masked_scores(t, k)
                    residual()
                    statistics(t, k)
                    lower_context()
                    stack_odd(1)
                    reciprocals(0)
                    stack_even(1)
                    reciprocals(1)
                    qk_lower(2)
                elif j == 2:
                    residual()
                    masked_scores(t, k)
                    lower_h(NORM - 1)
                    statistics(t, k)
                    lower_context()
                    stack_odd(2)
                    qk_lower(3)
                    reciprocals(0)
                    reciprocals(1)
                    stack_even(2)
                    stack_odd(3)
                    stack_even(3)
                    lower_h(NORM)
                    qk_lower(4)
                elif j == 3:
                    residual()
                    masked_scores(t, k)
                    statistics(t, k)
                    qk_lower(5)
                    lower_context()
                    stack_odd(5)
                    stack_even(5)
                    reciprocals(0)
                    stack_odd(4)
                    reciprocals(1)
                    stack_even(4)
                    lower_h(NORM)

            slots(dve, slot, weights)

        @block.gpsimd
        def _(pool):
            nc.gpsimd.memset(ident[:, :], 0.0).then_inc(pool_const, 1)
            nc.gpsimd.memset(ones[:, :], 1.0).then_inc(pool_const, 1)
            nc.gpsimd.memset(minus_half[:, :], -0.5).then_inc(pool_const, 1)
            pool.wait_ge(pool_const, 3)
            nc.gpsimd.affine_select(out=ident[:, :], in_=ident[:, :], compare_op=ALU.not_equal, fill=1.0, base=0,
                                    pattern=[[-1, 128]], channel_multiplier=1).then_inc(pool_const, 1)
            pool.wait_ge(pool_const, 4)
            RMAX = bass.bass_isa.ReduceOp.max

            def weights(t):
                if t == -4:
                    pool.wait_ge(vf_bias_loaded, 32)
                    nc.gpsimd.tensor_copy(bv_wide[:, :, :], bv_col[:, :].unsqueeze(2).to_broadcast([128, KT, 128])
                                          ).then_inc(bv_ready, 1)
                if t == -5:
                    pool.wait_ge(scale_step, 4)
                    nc.gpsimd.partition_all_reduce(largest_all[:, :], largest[:, :, 2], 128, RMAX
                                                   ).then_inc(largest_ready, 1)

            def slot(t, k):
                if isinstance(t, int) and t == -XB:
                    pool.wait_ge(ob_ready, 1)
                if valid(t + XB):
                    wait(pool, h_ready, t + XB + 1)
                    wait(pool, y_ready, t - 2)
                if valid(t + STATS):
                    wait(pool, moments_ready, t + STATS + 1)
                    wait(pool, h_ready, t + STATS - 1)
                if valid(t + 1):
                    pu, ju = group_of(t + 1, k + 1)
                    if ju == 0:
                        wait(pool, adj_loaded[pu], 2 * (t + 1 - pu * GROUP) + 16)
                    wait(pool, masked, 2 * t)

                if valid(t + XB):
                    r = (k + XB) % RING
                    nc.gpsimd.tensor_tensor(x_bias[:, r, :], x_in[:, r, :], out_bias[:, :], ALU.add
                                            ).then_inc(xb_ready, 1)

                if valid(t + STATS):
                    u, b = t + STATS, (k + STATS) % 2
                    nc.gpsimd.tensor_scalar(rstd[:, b, 0:1], moments[:, b, 1:2], EPS, None, ALU.add
                                            ).then_inc(rstd_step, 1)
                    nc.gpsimd.tensor_scalar(shift[:, b, 0:1], moments[:, b, 0:1], -1.0, None, ALU.mult
                                            ).then_inc(rstd_step, 1)

                if valid(t + 1):
                    nc.gpsimd.tensor_scalar(mask[:, (k + 1) % 2, :], adj_in[:, pu, ju, :], -NEG, NEG,
                                            ALU.mult, ALU.add).then_inc(mask_ready, 1)

                if valid(t + STATS):
                    pool.wait_ge(rstd_step, 3 * u + 2)
                    nc.gpsimd.tensor_tensor(rstd[:, b, 1:2], rstd[:, b, 0:1], minus_half[:, :], ALU.pow
                                            ).then_inc(rstd_step, 1)
                    pool.wait_ge(rstd_step, 3 * u + 3)
                    nc.gpsimd.tensor_tensor(shift[:, b, 1:2], shift[:, b, 0:1], rstd[:, b, 1:2], ALU.mult
                                            ).then_inc(norm_ready, 1)

                if valid(t):
                    b = k % 2
                    for odd in range(2):
                        half = slice(odd * PAIRS, (odd + 1) * PAIRS)
                        wait(pool, inv_ready, 2 * t + 1 + odd)
                        nc.gpsimd.tensor_tensor(s[:, b, half, :], s[:, b, half, :],
                                                inv_sums[:, b, half].unsqueeze(2).to_broadcast([128, PAIRS, NODES]),
                                                ALU.mult).then_inc(probs_ready, 1)

            slots(pool, slot, weights)


_INS = ["x", "adj"] + [f"L0_gnn_{n}" for n in ("Wq", "bq", "Wk", "bk", "Wv", "bv", "Wf", "bf")]


def kernel(**inputs):
    import numpy as _np
    import concourse.bacc as _bacc
    from concourse import mybir as _mybir
    from concourse.bass_utils import run_bass_kernel_spmd as _run

    nc = _bacc.Bacc("TRN2", target_bir_lowering=False, num_devices=1)
    arrays, args = {}, []
    for name in _INS:
        a = _np.ascontiguousarray(inputs[name])
        arrays[f"in_{name}"] = a
        args.append(nc.dram_tensor(f"in_{name}", a.shape, _mybir.dt.from_np(a.dtype), kind="ExternalInput").ap())
    shape = inputs["x"].shape
    args.append(nc.dram_tensor("out_0", shape, _mybir.dt.float32, kind="ExternalOutput").ap())
    graph_attention(nc, *args)
    r = _run(nc, [arrays], core_ids=[0])
    return r.results[0]["out_0"]
```
